# Optimizing a Trainium2 kernel written in Bass

```python
import numpy as np
import jax
import jax.numpy as jnp

def _softmax(x, axis=-1):
    return jax.nn.softmax(x, axis=axis)

def _gelu(x):
    return jax.nn.gelu(x, approximate=True)

def _silu(x):
    return jax.nn.silu(x)

def _sigmoid(x):
    return jax.nn.sigmoid(x)

def _layernorm(x, axis=-1, eps=1e-05):
    m = jnp.mean(x, axis=axis, keepdims=True)
    v = jnp.var(x, axis=axis, keepdims=True)
    return (x - m) / jnp.sqrt(v + eps)

def _scatter_add(tgt, idx, src, axis=0):
    return tgt.at[idx].add(src)

def _segment_sum(src, seg, n):
    return jax.ops.segment_sum(src, seg, n)
kernel_name = 'mk_gnn_ffn_d1_gnn_r8_6b3d60'

def setup_inputs(seed: int=0):
    np.random.seed(seed)
    _w = jnp.asarray

    def _rec_inputs():
        import jax
        import jax.numpy as jnp
        _gk = jax.random.key(seed)
        x = -0.0002117 + 1 * jax.random.normal(jax.random.fold_in(_gk, 1), (6250, 256), jnp.float32)
        src = jax.random.randint(jax.random.fold_in(_gk, 2), (100000,), 0, 6250, jnp.int32)
        dst = jnp.minimum((6250 * jax.random.uniform(jax.random.fold_in(_gk, 3), (100000,)) ** 2.0).astype(jnp.int32), 49999)
        _o = jnp.argsort(dst, stable=True)
        src = src[_o]
        dst = dst[_o]
        edge_weight = jax.random.uniform(jax.random.fold_in(_gk, 13), (100000,), jnp.float32, 0.0, 0.999994)
        return (x, src, dst, edge_weight)
    x, src, dst, edge_weight = _rec_inputs()

    def _L0_gnn_setup():
        import jax, jax.numpy as jnp
        import numpy as np
        NEG_SLOPE = 0.01

        def _leaky(x):
            return jnp.where(x >= 0, x, NEG_SLOPE * x)

        def _gcn(x, W, b, src, dst, w, n):
            h = x @ W
            agg = jax.ops.segment_sum(w[:, None] * h[src], dst, num_segments=n)
            return agg + b
        key = jax.random.key(seed)
        ks = jax.random.split(key, 10)
        N, E, IN, HID, OUT, B = (12500, 37500, 256, 256, 256, 128)
        features = jax.random.normal(ks[0], (N, IN), dtype=jnp.float32)
        values = jax.random.uniform(ks[1], (E,), dtype=jnp.float32)
        s = 1.0 / np.sqrt(IN)
        W1 = jax.random.normal(ks[2], (IN, HID), dtype=jnp.float32) * s
        b1 = jnp.zeros((HID,), dtype=jnp.float32)
        W2 = jax.random.normal(ks[3], (HID + IN, OUT), dtype=jnp.float32) * (1.0 / np.sqrt(HID + IN))
        b2 = jnp.zeros((OUT,), dtype=jnp.float32)
        Wl = jax.random.normal(ks[4], (HID + OUT, IN), dtype=jnp.float32) * (1.0 / np.sqrt(HID + OUT))
        bl = jnp.zeros((IN,), dtype=jnp.float32)
        adjs = jax.random.randint(ks[5], (2, E), 0, N, dtype=jnp.int64)
        batch = jnp.sort(jax.random.randint(ks[6], (N,), 0, B, dtype=jnp.int64))
        root_idx = jax.random.randint(ks[7], (B,), 0, N, dtype=jnp.int64)
        return {'features': features, 'values': values, 'W1': W1, 'b1': b1, 'W2': W2, 'b2': b2, 'Wl': Wl, 'bl': bl, 'adjs': adjs, 'batch': batch, 'root_idx': root_idx}
    _L0_gnn_all = _L0_gnn_setup()
    _L0_gnn_in = {k: v for k, v in _L0_gnn_all.items() if k in ('W1', 'b1', 'W2', 'b2', 'Wl', 'bl', 'root_idx')}
    del _L0_gnn_all

    def _L0_ffn_setup():
        import jax, jax.numpy as jnp
        import numpy as np
        B, S, D = (8, 512, 256)
        H = 4 * D
        CAPACITY = 0.5
        key = jax.random.key(seed)
        ks = jax.random.split(key, 6)
        x = jax.random.normal(ks[0], (B, S, D), dtype=jnp.float32)
        attention_mask = jnp.zeros((B, 1, 1, S), dtype=jnp.float32)
        wr = jax.random.normal(ks[1], (D, 1), dtype=jnp.float32) * 0.02
        br = jnp.zeros((1,), dtype=jnp.float32)
        w1 = jax.random.normal(ks[2], (D, H), dtype=jnp.float32) * 0.02
        b1 = jnp.zeros((H,), dtype=jnp.float32)
        w2 = jax.random.normal(ks[3], (H, D), dtype=jnp.float32) * 0.02
        b2 = jnp.zeros((D,), dtype=jnp.float32)
        return {'x': x, 'attention_mask': attention_mask, 'wr': wr, 'br': br, 'w1': w1, 'b1': b1, 'w2': w2, 'b2': b2}
    _L0_ffn_all = _L0_ffn_setup()
    _L0_ffn_in = {k: v for k, v in _L0_ffn_all.items() if k in ('attention_mask', 'wr', 'br', 'w1', 'b1', 'w2', 'b2')}
    del _L0_ffn_all
    return {'x': x, 'src': src, 'dst': dst, 'edge_weight': edge_weight, 'L0_gnn_W1': _L0_gnn_in['W1'], 'L0_gnn_b1': _L0_gnn_in['b1'], 'L0_gnn_W2': _L0_gnn_in['W2'], 'L0_gnn_b2': _L0_gnn_in['b2'], 'L0_gnn_Wl': _L0_gnn_in['Wl'], 'L0_gnn_bl': _L0_gnn_in['bl'], 'L0_gnn_root_idx': _L0_gnn_in['root_idx'], 'L0_ffn_attention_mask': _L0_ffn_in['attention_mask'], 'L0_ffn_wr': _L0_ffn_in['wr'], 'L0_ffn_br': _L0_ffn_in['br'], 'L0_ffn_w1': _L0_ffn_in['w1'], 'L0_ffn_b1': _L0_ffn_in['b1'], 'L0_ffn_w2': _L0_ffn_in['w2'], 'L0_ffn_b2': _L0_ffn_in['b2']}

def reference(x, src, dst, edge_weight, L0_gnn_W1, L0_gnn_b1, L0_gnn_W2, L0_gnn_b2, L0_gnn_Wl, L0_gnn_bl, L0_gnn_root_idx, L0_ffn_attention_mask, L0_ffn_wr, L0_ffn_br, L0_ffn_w1, L0_ffn_b1, L0_ffn_w2, L0_ffn_b2):
    import jax
    import jax.numpy as jnp

    def _L0_gnn_ref(features, values, W1, b1, W2, b2, Wl, bl, adjs, batch, root_idx):
        import jax, jax.numpy as jnp
        import numpy as np
        NEG_SLOPE = 0.01

        def _leaky(x):
            return jnp.where(x >= 0, x, NEG_SLOPE * x)

        def _gcn(x, W, b, src, dst, w, n):
            h = x @ W
            agg = jax.ops.segment_sum(w[:, None] * h[src], dst, num_segments=n)
            return agg + b
        N = features.shape[0]
        src, dst = (adjs[0], adjs[1])
        f1 = features
        h = _gcn(f1, W1, b1, src, dst, values, N)
        f2 = h
        root1 = f1[root_idx[batch]]
        x = _leaky(jnp.concatenate([h, root1], axis=1))
        x = _gcn(x, W2, b2, src, dst, values, N)
        x = _leaky(x)
        root2 = f2[root_idx[batch]]
        x = jnp.concatenate([x, root2], axis=1)
        return _leaky(x @ Wl + bl)

    def _L0_ffn_ref(x, attention_mask, wr, br, w1, b1, w2, b2):
        import jax, jax.numpy as jnp
        import numpy as np
        B, S, D = (8, 512, 256)
        H = 4 * D
        CAPACITY = 0.5
        b, s, d = x.shape
        weights = (jnp.einsum('bsd,do->bso', x, wr) + br)[..., 0]
        k = max(1, int(CAPACITY * s))
        kk = k - 1 if k > 1 else 1
        _, idx = jax.lax.top_k(weights, k)
        sel_idx = idx[:, :kk]
        sel = jnp.take_along_axis(x, sel_idx[:, :, None], axis=1)
        h = jax.nn.gelu(jnp.einsum('bkd,dh->bkh', sel, w1) + b1)
        y = jnp.einsum('bkh,hd->bkd', h, w2) + b2
        w_sel = jnp.take_along_axis(weights, sel_idx, axis=1)
        y = y * w_sel[..., None]
        batch_idx = jnp.arange(b)[:, None]
        processed = jnp.zeros_like(x).at[batch_idx, sel_idx].set(y)
        return processed + x
    edge_index = jnp.stack([src, dst])
    batch0 = jnp.zeros((6250,), jnp.int32)
    x = x + _L0_gnn_ref(_layernorm(x, axis=-1), edge_weight, L0_gnn_W1, L0_gnn_b1, L0_gnn_W2, L0_gnn_b2, L0_gnn_Wl, L0_gnn_bl, edge_index, batch0, L0_gnn_root_idx)
    x = x + _L0_ffn_ref(_layernorm(x, axis=-1)[None], L0_ffn_attention_mask, L0_ffn_wr, L0_ffn_br, L0_ffn_w1, L0_ffn_b1, L0_ffn_w2, L0_ffn_b2)[0]
    return x

_drawn_inputs = setup_inputs


def setup_inputs(seed=0):
    import zlib

    import numpy as np

    out = dict(_drawn_inputs(seed))
    spreads = {'L0_gnn_b1': (0.0, 0.1),
     'L0_gnn_b2': (0.0, 0.8),
     'L0_gnn_bl': (0.0, 0.42),
     'L0_ffn_b1': (0.0, 0.8),
     'L0_ffn_b2': (0.0, 0.8)}
    factors = {'L0_ffn_wr': 8.0, 'L0_ffn_w1': 8.0, 'L0_ffn_w2': 8.0}
    for name, (base, spread) in spreads.items():
        noise = np.random.default_rng([zlib.crc32(name.encode()), seed]).standard_normal(out[name].shape)
        drawn = base * np.exp(spread * noise) if base else spread * noise
        out[name] = jnp.asarray(drawn.astype(out[name].dtype))
    for name, factor in factors.items():
        out[name] = (out[name] * factor).astype(out[name].dtype)
    return out
```

```python
import concourse.bass as bass
from concourse import mybir
from contextlib import ExitStack


class Links:

    def __init__(self, engine, sem, start=0):
        self.engine, self.sem, self.start, self.steps = engine, sem, start, 0

    def __call__(self, instruction):
        self.steps += 1
        instruction.then_inc(self.sem, 1)
        self.engine.wait_ge(self.sem, self.start + self.steps)


def gnn_ffn_kernel(nc, x, src, dst, edge_weight, W1, b1, W2, b2, Wl, bl, root_idx,
                   wr, br, fw1, fb1, fw2, fb2, out):
    f32, i32, i16, bf16 = mybir.dt.float32, mybir.dt.int32, mybir.dt.int16, mybir.dt.bfloat16
    ALU, ACT, AX = mybir.AluOpType, mybir.ActivationFunctionType, mybir.AxisListType
    ds = bass.ds

    P = 128
    N, D = x.shape
    E = src.shape[0]
    HID = fw1.shape[1]
    KC = D // P
    HC = HID // P
    UB = 2
    HB = HC // UB
    NW = -(-N // P)
    LAST_ROWS = N - (NW - 1) * P
    SKEW = 2
    NI = NW + SKEW
    TG = 4
    GE = TG * P
    NG = -(-E // GE)
    NT = NG * TG
    RING = 16
    RG = RING // TG
    HALF = RING // 2
    NIT = NT // RING
    CH = 7
    CR = NT // CH
    GR = NG // 2
    ACC0 = SKEW
    DUMMY = NI + ACC0
    NACC = DUMMY + 1
    X0 = 1
    NX = NW + 2
    TOPK = max(1, int(0.5 * N)) - 1
    NPAD = NW * P
    EPS = 1e-5
    SLOPE = 0.01
    MAGIC = float(0x5F3759DF)
    NEWTON = 3
    LOWEST = -3.0e38
    assert NT == CH * CR and NG == 2 * GR and NT % RING == 0 and CR <= P and GR <= P

    f_dram = nc.dram_tensor("normed_rows", (NPAD, D), f32).ap()
    agg_dram = nc.dram_tensor("aggregate_rows", (NI * P, D), f32).ap()
    t2_dram = nc.dram_tensor("conv2_rows", (NI * P, D), f32).ap()

    ctx = ExitStack()
    with ctx:
        ctx.enter_context(nc.allow_non_contiguous_dma("small bias columns"))

        def sb(name, shape, dt=f32):
            return ctx.enter_context(nc.sbuf_tensor(name, shape, dt))

        def pb(name, shape, dt=f32):
            return ctx.enter_context(nc.psum_tensor(name, shape, dt))

        def sem(name):
            return ctx.enter_context(nc.semaphore(name))

        acc = sb("acc", [P, NACC, D])
        xs = sb("xs", [P, NX, D])
        ring = sb("ring", [P, RING, D])
        iota = sb("iota", [P, NPAD], i16)
        idx = sb("idx", [P, 2, NT + RING], i32)
        idx_stage = sb("idx_stage", [P, 2, HALF], i32)
        dstc = sb("dstc", [P, NT])
        wc = sb("wc", [P, NT])
        S = sb("S", [P, TG, P])
        W1s = sb("W1s", [P, KC, D])
        W2s = sb("W2s", [P, 2 * KC, D])
        Wls = sb("Wls", [P, 2 * KC, D])
        fw1s = sb("fw1s", [P, KC, HID])
        fw2s = sb("fw2s", [P, HC, D])
        b1c = sb("b1c", [P, KC])
        b2c = sb("b2c", [P, KC])
        fb1c = sb("fb1c", [P, HC])
        wrc = sb("wrc", [P, KC])
        brc = sb("brc", [P, 1])
        blb = sb("blb", [P, D])
        fb2b = sb("fb2b", [P, D])
        rootrow = sb("rootrow", [P, D])
        rooti = sb("rooti", [P, 3], i32)
        rootG = sb("rootG", [P, D])
        rootT = sb("rootT", [P, KC, P])
        root2T = sb("root2T", [P, KC, P])
        stage = sb("stage", [P, D])
        aggT = sb("aggT", [P, KC, P])
        yT = sb("yT", [P, KC, P])
        zT = sb("zT", [P, KC, P])
        rows = sb("rows", [P, D])
        vrow = sb("vrow", [P, D])
        xn = sb("xn", [P, D])
        xnT = sb("xnT", [P, KC, P])
        hT = sb("hT", [P, HC, P])
        ident = sb("ident", [P, P])
        ones = sb("ones", [P, P])
        lower = sb("lower", [P, P])
        zeros = sb("zeros", [P, D])
        mv = sb("mv", [P, NW, 2])
        bst = sb("bst", [P, NW, 6])
        ve = sb("ve", [P, NW])
        nh = sb("nh", [P, NW])
        ta = sb("ta", [P, NW])
        rstd = sb("rstd", [P, NW])
        wt = sb("wt", [P, NI])
        ctab = sb("ctab", [1, NG + 4], i32)
        ltab = sb("ltab", [1, NG], i32)
        gtab = sb("gtab", [1, 65], i32)
        nmax = sb("gmm", [P, 2, 2], i32)
        glo = sb("glo", [P, 2, 2])
        gcnt = sb("gcnt", [P, 2])
        diag = sb("diag", [P, 2, 2, GR])
        gcol = sb("gcol", [64, NG])
        wcol = sb("wcol", [64, 1])
        gnum = sb("gnum", [64, NG])
        gd = sb("gd", [64, 1])
        cumf = sb("cumf", [1, NG])
        zrow = sb("zrow", [1, NG])
        thr = sb("thr", [P, 2], i32)
        bit = sb("bit", [P, 1], i32)
        sel = sb("sel", [P, 1], i32)
        small = sb("small", [P, 8])
        us = sb("us", [P, NW])
        scr = sb("scr", [P, NW])
        mgt = sb("mgt", [P, NW])
        mtie = sb("mtie", [P, NW])
        mw = sb("mw", [P, NW])

        rflat = ring[:, :, :].rearrange("p r d -> p (r d)")
        EW = CH * P
        src_rows = rflat[0:CR, 0:EW].bitcast(i32).rearrange("p (c e) -> p c e", c=CH)
        dst_rows = rflat[0:CR, EW:2 * EW].bitcast(i32).rearrange("p (c e) -> p c e", c=CH)
        w_rows = rflat[0:CR, 2 * EW:3 * EW].rearrange("p (c e) -> p c e", c=CH)
        src_rowsf = rflat[0:CR, 0:EW].rearrange("p (c e) -> p c e", c=CH)
        dst_rowsf = rflat[0:CR, EW:2 * EW].rearrange("p (c e) -> p c e", c=CH)
        dst_groups = rflat[0:GR, 3 * EW:3 * EW + 2 * GE].bitcast(i32).rearrange("p (c e) -> p c e", c=2)

        ps_agg = pb("ps_agg", [P, 2, 512])
        ps_t = pb("ps_t", [P, 512])
        ps_h = pb("ps_h", [P, 512])
        ps_o = pb("ps_o", [P, 512])
        ps_up = pb("ps_up", [P, HC, P])
        ps_dn = pb("ps_dn", [P, 512])
        up_flat = ps_up[:, :, :].rearrange("p c n -> p (c n)")

        edges_cleared, edges_loaded = sem("edges_cleared"), sem("edges_loaded")
        rows_floated, edges_turned, edges_kept = sem("rows_floated"), sem("edges_turned"), sem("edges_kept")
        groups_loaded = sem("groups_loaded")
        xs_cleared = sem("xs_cleared")
        XCH = [(0, 12), (12, 24), (24, 36), (36, NW)]
        x_loaded = [sem(f"x_loaded{c}") for c in range(len(XCH))]
        stats_ready = sem("stats_ready")
        f_dve, f_pool, f_stored = sem("f_dve"), sem("f_pool"), sem("f_stored")
        weights_loaded, consts_ready, pool_chain = sem("weights_loaded"), sem("consts_ready"), sem("pool_chain")
        dve_chain = sem("dve_chain")
        diag_ready, spread_done, gd_ready, gd_turned = sem("diag_ready"), sem("spread_done"), sem("gd_ready"), sem("gd_turned")
        tables_ready = sem("tables_ready")
        root_loaded, root_ready, root_gathered = sem("root_loaded"), sem("root_ready"), sem("root_gathered")
        root_turned, root_kept, root_done, rootrow_ready = sem("root_turned"), sem("root_kept"), sem("root_done"), sem("rootrow_ready")
        root2_h, root2_kept = sem("root2_h"), sem("root2_kept")
        tile_sem = [sem(f"tile_gathered{k}") for k in range(RING)]
        idx_sem = [sem(f"idx_staged{h}") for h in range(2)]
        L2 = range(2)
        landed = [sem(f"tiles_landed{l}") for l in L2]
        group_done = [sem(f"group_done{l}") for l in L2]
        s_ready = [sem(f"s_ready{l}") for l in L2]
        mm_done = [sem(f"mm_done{l}") for l in L2]
        acc_step = [sem(f"acc_step{l}") for l in L2]
        flushed = [sem(f"flushed{l}") for l in L2]
        staged = [sem(f"staged{l}") for l in L2]
        t_done = [sem(f"t_done{l}") for l in L2]
        aggT_ready = sem("aggT_ready")
        h_done = sem("h_done")
        y_ready = [sem(f"y_ready{l}") for l in L2]
        z_ready = [sem(f"z_ready{l}") for l in L2]
        o_done = [sem(f"o_done{l}") for l in L2]
        o_kept = [sem(f"o_kept{l}") for l in L2]
        t2_stored, agg_stored = sem("t2_stored"), sem("agg_stored")
        acc_cleared = sem("acc_cleared")
        stats_held, gather_held = sem("stats_held"), sem("gather_held")
        ln_chain = sem("ln_chain")
        xn_ready, xnT_done, xnT_ready = sem("xn_ready"), sem("xnT_done"), sem("xnT_ready")
        router_done, router_kept = sem("router_done"), sem("router_kept")
        up_done, gelu_done, down_done, down_kept = sem("up_done"), sem("gelu_done"), sem("down_done"), sem("down_kept")
        wt_masked, count_ready, count_done = sem("wt_masked"), sem("count_ready"), sem("count_done")
        bit_chain, tie_ready, tie_done = sem("bit_chain"), sem("tie_ready"), sem("tie_done")
        sel_chain, out_ready, out_stored = sem("sel_chain"), sem("out_ready"), sem("out_stored")
        N_WEIGHTS = 12
        OUTCH = [(i, min(i + 7, NW)) for i in range(0, NW, 7)]

        block = ctx.enter_context(nc.Block())

        @block.sync
        def _(sp):
            full = (CH - 1) * CR * P
            part = (E - full) // P
            rest = E - full - part * P
            sp.wait_ge(edges_cleared, 4)
            for a, r in ((src, src_rows), (dst, dst_rows), (edge_weight, w_rows)):
                sp.dma_start(r[:, 0:CH - 1, :], a[0:full].rearrange("(c r e) -> r c e", r=CR, e=P)).then_inc(edges_loaded, 16)
                sp.dma_start(r[0:part, CH - 1, :], a[full:full + part * P].rearrange("(r e) -> r e", e=P)).then_inc(edges_loaded, 16)
                sp.dma_start(r[part:part + 1, CH - 1, 0:rest], a[full + part * P:E].rearrange("(r e) -> r e", r=1)).then_inc(edges_loaded, 16)
            gfull = E // GE - GR
            gend = (GR + gfull) * GE
            sp.dma_start(dst_groups[:, 0, :], dst[0:GR * GE].rearrange("(r e) -> r e", e=GE)).then_inc(groups_loaded, 16)
            sp.dma_start(dst_groups[0:gfull, 1, :], dst[GR * GE:gend].rearrange("(r e) -> r e", e=GE)).then_inc(groups_loaded, 16)
            sp.dma_start(dst_groups[gfull:gfull + 1, 1, 0:E - gend], dst[gend:E].rearrange("(r e) -> r e", r=1)).then_inc(groups_loaded, 16)
            sp.wait_ge(xs_cleared, 1)
            for c, (w0, w1) in enumerate(XCH):
                wf = min(w1, NW - 1)
                sp.dma_start(xs[:, X0 + w0:X0 + wf, :], x[w0 * P:wf * P, :].rearrange("(w p) d -> p w d", p=P)).then_inc(x_loaded[c], 16)
            sp.dma_start(xs[0:LAST_ROWS, X0 + NW - 1, :], x[(NW - 1) * P:N, :]).then_inc(x_loaded[-1], 16)
            for c, (w0, w1) in enumerate(XCH):
                sp.wait_ge(f_dve, c + 1)
                sp.wait_ge(f_pool, c + 1)
                sp.dma_start(f_dram[w0 * P:w1 * P, :].rearrange("(w p) d -> p w d", p=P), acc[:, ACC0 + w0:ACC0 + w1, :]).then_inc(f_stored, 16)
            sp.wait_ge(edges_kept, 3)
            for l in L2:
                for h in range(2):
                    sp.dma_start(idx_stage[:, h, :], idx[:, l, h * HALF:(h + 1) * HALF]).then_inc(idx_sem[h], 16)
                with sp.Fori(0, NIT) as it:
                    for k in range(RING):
                        sp.wait_ge(tile_sem[k], 16 * (it + (NIT * l + 1)))
                        sp.sem_inc(landed[l], 1)
                        if k % HALF == HALF - 1:
                            h = k // HALF
                            sp.dma_start(idx_stage[:, h, :], idx[:, l, ds((it + 1) * RING + h * HALF, HALF)]).then_inc(idx_sem[h], 16)
                for h in range(2):
                    sp.wait_ge(idx_sem[h], 16 * (NIT + 1) * (l + 1))
            for c, (w0, w1) in enumerate(OUTCH):
                sp.wait_ge(out_ready, c + 1)
                wf = min(w1, NW - 1)
                sp.dma_start(out[w0 * P:wf * P, :].rearrange("(w p) d -> p w d", p=P), xs[:, X0 + w0:X0 + wf, :]).then_inc(out_stored, 16)
                if w1 == NW:
                    sp.dma_start(out[(NW - 1) * P:N, :], xs[0:LAST_ROWS, X0 + NW - 1, :]).then_inc(out_stored, 16)
            sp.wait_ge(out_stored, 16 * (len(OUTCH) + 1))

        @block.gpsimd
        def _(pool):
            link = Links(pool, pool_chain)
            nc.gpsimd.memset(src_rows[:, CH - 1, :], 0).then_inc(edges_cleared, 1)
            nc.gpsimd.memset(dst_rows[:, CH - 1, :], N - 1).then_inc(edges_cleared, 1)
            nc.gpsimd.memset(w_rows[:, CH - 1, :], 0.0).then_inc(edges_cleared, 1)
            nc.gpsimd.memset(dst_groups[:, 1, :], N - 1).then_inc(edges_cleared, 1)
            link(nc.gpsimd.memset(ident[:, :], 0.0))
            nc.gpsimd.affine_select(out=ident[:, :], in_=ident[:, :], compare_op=ALU.not_equal, fill=1.0, base=0,
                                    pattern=[[-1, P]], channel_multiplier=1).then_inc(consts_ready, 1)
            link(nc.gpsimd.memset(lower[:, :], 1.0))
            nc.gpsimd.affine_select(out=lower[:, :], in_=lower[:, :], compare_op=ALU.is_gt, fill=0.0, base=0,
                                    pattern=[[1, P]], channel_multiplier=-1).then_inc(consts_ready, 1)
            nc.gpsimd.iota(iota[:, :], pattern=[[1, NPAD]], base=0, channel_multiplier=0).then_inc(consts_ready, 1)
            pool.wait_ge(edges_loaded, 16 * 9)
            nc.gpsimd.tensor_copy(src_rowsf[:, :, :], src_rows[:, :, :]).then_inc(rows_floated, 1)
            nc.gpsimd.tensor_copy(dst_rowsf[:, :, :], dst_rows[:, :, :]).then_inc(rows_floated, 1)
            for c, (w0, w1) in enumerate(XCH):
                pool.wait_ge(stats_ready, c + 1)
                for w in range(w0 + 1, w1, 2):
                    last = nc.gpsimd.tensor_scalar(acc[:, ACC0 + w, :], xs[:, X0 + w, :], mv[:, w, 0:1], rstd[:, w:w + 1], ALU.subtract, ALU.mult)
                last.then_inc(f_pool, 1)
            for l in L2:
                pool.wait_ge(root_ready, 1)
                if l == 0:
                    pool.wait_ge(f_stored, 16 * len(XCH))
                else:
                    pool.wait_ge(agg_stored, 16 * (NI + 1))
                    pool.wait_ge(t2_stored, 16 * (NI + 1))
                    pool.wait_ge(root_turned, 1)
                pool.indirect_dma_start(out=rootG[:, :], out_offset=None, in_=f_dram if l == 0 else agg_dram,
                                        in_offset=bass.IndirectOffsetOnAxis(ap=rooti[:, 2:3], axis=0)).then_inc(root_gathered, 16)
                with pool.Fori(0, NIT) as it:
                    for k in range(RING):
                        if k % HALF == 0:
                            pool.wait_ge(idx_sem[k // HALF], 16 * (it + ((NIT + 1) * l + 1)))
                        if k % TG == 0:
                            pool.wait_ge(group_done[l], RG * it + (k // TG + 2))
                            pool.sem_inc(gather_held, 1)
                        pool.indirect_dma_start(out=ring[:, k, :], out_offset=None, in_=f_dram if l == 0 else t2_dram,
                                                in_offset=bass.IndirectOffsetOnAxis(ap=idx_stage[:, k // HALF, k % HALF:k % HALF + 1], axis=0)).then_inc(tile_sem[k], 16)
            pool.wait_ge(router_kept, NI + 1)
            nc.gpsimd.affine_select(out=wt[:, SKEW:NI], in_=wt[:, SKEW:NI], compare_op=ALU.is_ge, fill=LOWEST, base=N - 1,
                                    pattern=[[-P, NW]], channel_multiplier=-1).then_inc(wt_masked, 1)

        @block.scalar
        def _(act):
            col = "(c p) -> p c"
            one = "(o n) -> o n"
            loads = [
                (W1s[:, :, :], W1.rearrange("(k p) n -> p k n", p=P)),
                (W2s[:, :, :], W2.rearrange("(k p) n -> p k n", p=P)),
                (Wls[:, :, :], Wl.rearrange("(k p) n -> p k n", p=P)),
                (fw1s[:, :, :], fw1.rearrange("(k p) n -> p k n", p=P)),
                (fw2s[:, :, :], fw2.rearrange("(k p) n -> p k n", p=P)),
                (b1c[:, :], b1.rearrange(col, p=P)),
                (b2c[:, :], b2.rearrange(col, p=P)),
                (fb1c[:, :], fb1.rearrange(col, p=P)),
                (wrc[:, :], wr.rearrange("(k p) o -> p (k o)", p=P)),
                (brc[:, :], br.rearrange(one, o=1).to_broadcast([P, 1])),
                (blb[:, :], bl.rearrange(one, o=1).to_broadcast([P, D])),
                (fb2b[:, :], fb2.rearrange(one, o=1).to_broadcast([P, D])),
            ]
            assert len(loads) == N_WEIGHTS
            act.dma_start(rooti[:, 0:1], root_idx[0:1].rearrange(one, o=1).to_broadcast([P, 1])).then_inc(root_loaded, 16)
            for to, of in loads:
                act.dma_start(to, of).then_inc(weights_loaded, 16)
            act.wait_ge(weights_loaded, 16 * N_WEIGHTS)

            act.sem_inc(aggT_ready, 1)
            act.sem_inc(y_ready[0], 1)
            act.sem_inc(staged[0], 1)
            with act.Fori(0, NI) as w:
                act.wait_ge(t_done[0], w + 2)
                act.wait_ge(h_done, w + 1)
                nc.scalar.activation(aggT[:, :, :].rearrange("p k n -> p (k n)"), ps_t[:, 0:D], ACT.Copy).then_inc(aggT_ready, 1)
                act.wait_ge(o_kept[0], w + 2)
                act.dma_start(t2_dram[ds(w * P, P), :], rows[:, :]).then_inc(t2_stored, 16)
                act.wait_ge(h_done, w + 2)
                act.wait_ge(z_ready[0], w + 1)
                for k in range(KC):
                    last = nc.scalar.activation(yT[:, k, :], ps_h[:, k * P:(k + 1) * P], ACT.Identity, bias=b1c[:, k:k + 1])
                last.then_inc(y_ready[0], 1)
                act.wait_ge(flushed[0], w + 1)
                act.wait_ge(t_done[0], w + 2)
                act.wait_ge(agg_stored, 16 * (w + 1))
                nc.scalar.activation(stage[:, :], acc[:, ds(w + ACC0, 1), :].rearrange("p a d -> p (a d)"), ACT.Copy).then_inc(staged[0], 1)
                act.wait_ge(staged[0], w + 2)
                act.dma_start(agg_dram[ds(w * P, P), :], stage[:, :]).then_inc(agg_stored, 16)

            act.wait_ge(agg_stored, 16 * (NI + 1))
            act.sem_inc(xnT_ready, 1)
            act.sem_inc(y_ready[1], 1)
            act.sem_inc(gelu_done, HC)
            act.sem_inc(staged[1], 1)
            with act.Fori(0, NI) as w:
                act.wait_ge(xnT_done, w + 2)
                act.wait_ge(up_done, UB * (w + 1))
                nc.scalar.activation(xnT[:, :, :].rearrange("p k n -> p (k n)"), ps_h[:, 0:D], ACT.Copy).then_inc(xnT_ready, 1)
                act.wait_ge(t_done[1], w + 2)
                act.wait_ge(z_ready[1], w + 1)
                for k in range(KC):
                    last = nc.scalar.activation(yT[:, k, :], ps_t[:, k * P:(k + 1) * P], ACT.Identity, bias=b2c[:, k:k + 1])
                last.then_inc(y_ready[1], 1)
                act.wait_ge(down_done, w + 1)
                for c in range(HC):
                    if c % HB == 0:
                        act.wait_ge(up_done, UB * w + (UB + c // HB + 1))
                    nc.scalar.activation(hT[:, c, :], ps_up[:, c, :], ACT.Gelu_apprx_tanh, bias=fb1c[:, c:c + 1]).then_inc(gelu_done, 1)
                act.wait_ge(flushed[1], w + 1)
                nc.scalar.activation(stage[:, :], acc[:, ds(w + ACC0, 1), :].rearrange("p a d -> p (a d)"), ACT.Copy).then_inc(staged[1], 1)

        @block.tensor
        def _(pe):
            pe.wait_ge(consts_ready, 6)
            pe.wait_ge(rows_floated, 2)
            pe.wait_ge(edges_loaded, 16 * 9)
            banks = [(ps_t[:, :], ps_h[:, :]), (ps_o[:, :], ps_dn[:, :]), (up_flat[:, 0:512], up_flat[:, 512:1024])]
            for r, (b0, b1_) in zip((src_rowsf, dst_rowsf, w_rows), banks):
                for c in range(CH):
                    to = b0[:, c * CR:(c + 1) * CR] if c < 4 else b1_[:, (c - 4) * CR:(c - 3) * CR]
                    last = nc.tensor.transpose(to, r[:, c, :], ident[0:CR, 0:CR])
                last.then_inc(edges_turned, 1)
            pe.wait_ge(diag_ready, 1)
            pe.wait_ge(edges_kept, 3)
            for i in range(2):
                to = (ps_t, ps_o)[i]
                last = nc.tensor.matmul(to[0:64, 0:NG], ones[0:GR, 0:64], diag[0:GR, i, :, :].rearrange("p c g -> p (c g)"), start=True, stop=True)
            last.then_inc(spread_done, 1)
            pe.wait_ge(gd_ready, 1)
            nc.tensor.matmul(ps_h[0:1, 0:64], gd[0:64, 0:1], ident[0:64, 0:64], start=True, stop=True).then_inc(gd_turned, 1)

            def turn_root(n):
                pe.wait_ge(root_gathered, 16 * n)
                for k in range(KC):
                    last = nc.tensor.transpose(ps_dn[:, k * P:(k + 1) * P], rootG[:, k * P:(k + 1) * P], ident[:, :])
                last.then_inc(root_turned, 1)
                pe.wait_ge(root_kept, n)

            def root_term(of, W):
                for k in range(KC):
                    last = nc.tensor.matmul(ps_dn[:, 0:D], of[:, k, :], W[:, KC + k, :], start=(k == 0), stop=(k == KC - 1))
                last.then_inc(root_done, 1)

            def edge_groups(l, w):
                g0 = pe.value_load(gtab[0:1, ds(w, 1)], min_val=0, max_val=NG)
                g1 = pe.value_load(gtab[0:1, ds(w + 1, 1)], min_val=0, max_val=NG)
                with pe.If(g0 < g1):
                    with pe.Fori(g0, g1) as g:
                        p0 = pe.value_load(ctab[0:1, ds(g, 1)], min_val=0, max_val=NG * NW)
                        p1 = pe.value_load(ctab[0:1, ds(g + 1, 1)], min_val=0, max_val=NG * NW)
                        with pe.Fori(p0, p1) as i:
                            pe.wait_ge(acc_step[l], i + w + 1)
                            for k in range(TG):
                                pe.wait_ge(landed[l], TG * g + (k + 1))
                                pe.wait_ge(s_ready[l], TG * i + (k + 1))
                                nc.tensor.matmul(ps_agg[:, ds(i % 2, 1), 0:D].rearrange("p a d -> p (a d)"), S[:, k, :],
                                                 ring[:, ds((g % RG) * TG + k, 1), :].rearrange("p a d -> p (a d)"),
                                                 start=(k == 0), stop=(k == TG - 1)).then_inc(mm_done[l], 1)

            pe.wait_ge(weights_loaded, 16 * N_WEIGHTS)
            turn_root(1)
            root_term(rootT, W2s)
            pe.wait_ge(rootrow_ready, 1)
            pe.wait_ge(tables_ready, 1)

            for s, n in ((t_done[0], 1), (h_done, 1), (o_done[0], 1), (mm_done[0], TG)):
                pe.sem_inc(s, n)
            with pe.Fori(0, NI) as w:
                pe.wait_ge(staged[0], w + 1)
                pe.wait_ge(aggT_ready, w + 1)
                for k in range(KC):
                    last = nc.tensor.transpose(ps_t[:, k * P:(k + 1) * P], stage[:, k * P:(k + 1) * P], ident[:, :])
                last.then_inc(t_done[0], 1)
                pe.wait_ge(z_ready[0], w + 1)
                pe.wait_ge(o_kept[0], w + 1)
                for k in range(KC):
                    last = nc.tensor.matmul(ps_o[:, 0:D], zT[:, k, :], W2s[:, k, :], start=(k == 0), stop=(k == KC - 1))
                last.then_inc(o_done[0], 1)
                edge_groups(0, w)
                pe.wait_ge(aggT_ready, w + 2)
                pe.wait_ge(y_ready[0], w + 1)
                for c in range(KC):
                    for k in range(KC):
                        last = nc.tensor.matmul(ps_h[:, c * P:(c + 1) * P], W1s[:, k, c * P:(c + 1) * P], aggT[:, k, :], start=(k == 0), stop=(k == KC - 1))
                last.then_inc(h_done, 1)

            pe.wait_ge(y_ready[0], NI + 1)
            for s, n in ((t_done[1], 1), (xnT_done, 1), (up_done, UB), (down_done, 1), (o_done[1], 1), (mm_done[1], TG)):
                pe.sem_inc(s, n)
            turn_root(2)
            for c in range(KC):
                for k in range(KC):
                    last = nc.tensor.matmul(ps_h[:, c * P:(c + 1) * P], W1s[:, k, c * P:(c + 1) * P], rootT[:, k, :], start=(k == 0), stop=(k == KC - 1))
            last.then_inc(root2_h, 1)
            pe.wait_ge(root2_kept, 1)
            root_term(root2T, Wls)
            pe.wait_ge(rootrow_ready, 2)
            with pe.Fori(0, NI) as w:
                pe.wait_ge(xn_ready, w + 1)
                pe.wait_ge(xnT_ready, w + 1)
                for k in range(KC):
                    last = nc.tensor.transpose(ps_h[:, k * P:(k + 1) * P], xn[:, k * P:(k + 1) * P], ident[:, :])
                last.then_inc(xnT_done, 1)
                pe.wait_ge(staged[1], w + 1)
                pe.wait_ge(y_ready[1], w + 1)
                for k in range(KC):
                    last = nc.tensor.transpose(ps_t[:, k * P:(k + 1) * P], stage[:, k * P:(k + 1) * P], ident[:, :])
                last.then_inc(t_done[1], 1)
                pe.wait_ge(xnT_ready, w + 2)
                pe.wait_ge(o_kept[1], w + 1)
                pe.wait_ge(router_kept, w + 1)
                for k in range(KC):
                    last = nc.tensor.matmul(ps_o[:, D:D + 1], xnT[:, k, :], wrc[:, k:k + 1], start=(k == 0), stop=(k == KC - 1))
                last.then_inc(router_done, 1)
                for c in range(HC):
                    if c % HB == 0:
                        pe.wait_ge(gelu_done, HC * w + (c + HB))
                    for k in range(KC):
                        last = nc.tensor.matmul(ps_up[:, c, :], fw1s[:, k, c * P:(c + 1) * P], xnT[:, k, :], start=(k == 0), stop=(k == KC - 1))
                    if c % HB == HB - 1:
                        last.then_inc(up_done, 1)
                edge_groups(1, w)
                pe.wait_ge(z_ready[1], w + 2)
                pe.wait_ge(router_kept, w + 2)
                for k in range(KC):
                    last = nc.tensor.matmul(ps_o[:, 0:D], zT[:, k, :], Wls[:, k, :], start=(k == 0), stop=(k == KC - 1))
                last.then_inc(o_done[1], 1)
                pe.wait_ge(down_kept, w + 1)
                for c in range(HC):
                    pe.wait_ge(gelu_done, HC * w + (HC + c + 1))
                    last = nc.tensor.matmul(ps_dn[:, 0:D], hT[:, c, :], fw2s[:, c, :], start=(c == 0), stop=(c == HC - 1))
                last.then_inc(down_done, 1)

            pe.wait_ge(down_kept, NI + 1)
            with pe.Fori(0, 33) as r:
                pe.wait_ge(count_ready, r + 1)
                nc.tensor.matmul(ps_o[:, 0:1], ones[:, :], small[:, 0:1], start=True, stop=True).then_inc(count_done, 1)
            pe.wait_ge(tie_ready, 1)
            nc.tensor.matmul(ps_t[:, 0:NW], lower[:, :], mtie[:, :], start=True, stop=True)
            nc.tensor.matmul(ps_h[:, 0:NW], ones[:, :], mtie[:, :], start=True, stop=True).then_inc(tie_done, 1)

        @block.vector
        def _(dve):
            V = nc.vector
            link = Links(dve, dve_chain)

            def inv_sqrt(link, var, ve, nh, ta, y):
                link(V.tensor_scalar(ve, var, EPS, None, ALU.add))
                link(V.tensor_scalar(y.bitcast(i32), ve.bitcast(i32), 1, None, ALU.logical_shift_right))
                link(V.tensor_scalar(y.bitcast(i32), y.bitcast(i32), -1.0, MAGIC, ALU.mult, ALU.add))
                link(V.tensor_scalar(nh, ve, -0.5, None, ALU.mult))
                for _ in range(NEWTON):
                    link(V.tensor_tensor(ta, y, y, op=ALU.mult))
                    link(V.tensor_tensor(ta, ta, nh, op=ALU.mult))
                    link(V.scalar_tensor_tensor(y, ta, 1.5, y, ALU.add, ALU.mult))

            LN_LINKS = 4 + 3 * NEWTON

            V.memset(xs[:, 0:X0, :], 0.0)
            V.memset(xs[:, X0 + NW - 1:NX, :], 0.0).then_inc(xs_cleared, 1)
            V.memset(ones[:, :], 1.0).then_inc(consts_ready, 1)
            V.memset(ps_agg[:, :, :], 0.0).then_inc(consts_ready, 1)
            for t in (zeros[:, :], stage[:, :], zT[:, :, :], xn[:, :], rows[:, :]):
                last = V.memset(t, 0.0)
            last.then_inc(consts_ready, 1)
            V.memset(idx[:, :, NT:NT + RING], 0)
            V.memset(zrow[:, :], 0.0)
            link(V.memset(gtab[:, :], 0))
            link(V.memset(ctab[:, :], 0))

            dve.wait_ge(groups_loaded, 16 * 3)
            link(V.tensor_reduce(nmax[0:GR, 0, :], dst_groups[:, :, :], AX.X, ALU.min))
            link(V.tensor_reduce(nmax[0:GR, 1, :], dst_groups[:, :, :], AX.X, ALU.max))
            link(V.tensor_scalar(nmax[0:GR, :, :], nmax[0:GR, :, :], 7, None, ALU.arith_shift_right))
            link(V.tensor_scalar(glo[0:GR, :, :], nmax[0:GR, :, :], 0.0, float(NW - 1), ALU.max, ALU.min))
            link(V.scalar_tensor_tensor(gcnt[0:GR, :], glo[0:GR, 1, :], 1.0, glo[0:GR, 0, :], ALU.add, ALU.subtract))
            dve.wait_ge(consts_ready, 6)
            for c in range(2):
                V.tensor_scalar(diag[0:GR, 0, c, :], ident[0:GR, 0:GR], glo[0:GR, 0, c:c + 1], None, ALU.mult)
                last = V.tensor_scalar(diag[0:GR, 1, c, :], ident[0:GR, 0:GR], gcnt[0:GR, c:c + 1], None, ALU.mult)
            last.then_inc(diag_ready, 1)

            dve.wait_ge(edges_turned, 3)
            c4 = 4 * CR
            for b, n, m in ((ps_t, 0, c4), (ps_h, c4, NT)):
                V.tensor_scalar(idx[:, 0, n:m], b[:, 0:m - n], 0.0, float(N - 1), ALU.max, ALU.min)
            link(V.tensor_copy(dstc[:, 0:c4], ps_o[:, 0:c4]))
            V.tensor_scalar(idx[:, 1, 0:NT], idx[:, 0, 0:NT], float(SKEW * P), None, ALU.add).then_inc(edges_kept, 1)
            V.tensor_copy(dstc[:, c4:NT], ps_dn[:, 0:NT - c4]).then_inc(edges_kept, 1)
            V.tensor_copy(wc[:, 0:c4], up_flat[:, 0:c4])
            V.tensor_copy(wc[:, c4:NT], up_flat[:, 512:512 + NT - c4]).then_inc(edges_kept, 1)

            dve.wait_ge(root_loaded, 16)
            link(V.tensor_scalar(rooti[:, 1:2], rooti[:, 0:1], 0.0, float(N), ALU.is_lt, ALU.mult))
            link(V.tensor_tensor(rooti[:, 1:2], rooti[:, 1:2], rooti[:, 0:1], op=ALU.add))
            V.tensor_scalar(rooti[:, 2:3], rooti[:, 1:2], 0.0, float(N - 1), ALU.max, ALU.min).then_inc(root_ready, 1)

            dve.wait_ge(spread_done, 1)
            link(V.tensor_tensor_scan(cumf[0:1, :], ps_o[0:1, 0:NG], zrow[0:1, :], 0.0, ALU.add, ALU.add))
            V.tensor_copy(ctab[0:1, 1:NG + 1], cumf[0:1, :])
            V.tensor_copy(ltab[0:1, :], ps_t[0:1, 0:NG])
            iw = iota[0:64, 0:NG]
            link(V.tensor_tensor(gnum[:, 0:64], iota[0:64, 0:64], ident[0:64, 0:64], op=ALU.mult))
            link(V.tensor_reduce(wcol[:, 0:1], gnum[:, 0:64], AX.X, ALU.add))
            link(V.tensor_scalar(gnum[:, :], iw, 1.0, None, ALU.add))
            link(V.scalar_tensor_tensor(gcol[:, :], ps_t[0:64, 0:NG], wcol[:, 0:1], gnum[:, :], ALU.is_le, ALU.mult))
            V.tensor_reduce(gd[:, 0:1], gcol[:, :], AX.X, ALU.max).then_inc(gd_ready, 1)
            dve.wait_ge(gd_turned, 1)
            V.tensor_copy(gtab[0:1, 1:65], ps_h[0:1, 0:64]).then_inc(tables_ready, 1)

            for c, (w0, w1) in enumerate(XCH):
                dve.wait_ge(x_loaded[c], 32 if w1 == NW else 16)
                for w in range(w0, w1):
                    last = V.bn_stats(bst[:, w, :], xs[:, X0 + w, :])
                link(last)
                for w in range(w0, w1):
                    last = V.bn_aggr(mv[:, w, :], bst[:, w, :])
                link(last)
                inv_sqrt(link, mv[:, w0:w1, 1:2].rearrange("p w o -> p (w o)"), ve[:, w0:w1], nh[:, w0:w1], ta[:, w0:w1], rstd[:, w0:w1])
                dve.sem_inc(stats_ready, 1)
                for w in range(w0, w1, 2):
                    last = V.tensor_scalar(acc[:, ACC0 + w, :], xs[:, X0 + w, :], mv[:, w, 0:1], rstd[:, w:w + 1], ALU.subtract, ALU.mult)
                last.then_inc(f_dve, 1)

            dve.wait_ge(f_stored, 16 * len(XCH))
            link(V.memset(acc[:, :, :], 0.0))

            pend = dve.alloc_register("pending_window")

            def leaky(to, of):
                return V.scalar_tensor_tensor(to, of, SLOPE, of, ALU.mult, ALU.max)

            def flat(t):
                return t.rearrange("p k n -> p (k n)")

            def add_pair(l, slot):
                at = nc.s_assert_within(dve.snap(pend), 0, NACC - 1, skip_runtime_bounds_check_because="only such windows and the dummy are moved into it")
                to = flat(acc[:, ds(at, 1), :])
                return V.tensor_tensor(to, to, flat(ps_agg[:, ds(slot, 1), 0:D]), op=ALU.add)

            def edge_groups(l, w):
                g0 = dve.value_load(gtab[0:1, ds(w, 1)], min_val=0, max_val=NG)
                g1 = dve.value_load(gtab[0:1, ds(w + 1, 1)], min_val=0, max_val=NG)
                with dve.If(g0 < g1):
                    with dve.Fori(g0, g1) as g:
                        p0 = dve.value_load(ctab[0:1, ds(g, 1)], min_val=0, max_val=NG * NW)
                        p1 = dve.value_load(ctab[0:1, ds(g + 1, 1)], min_val=0, max_val=NG * NW)
                        lo = dve.value_load(ltab[0:1, ds(g, 1)], min_val=0, max_val=NW - 1)
                        with dve.Fori(p0, p1) as i:
                            win = nc.s_assert_within(dve.snap(lo + i - p0), 0, NW - 1, skip_runtime_bounds_check_because="the tables hold windows clamped to this range")
                            for k in range(TG):
                                dve.wait_ge(mm_done[l], TG * i + (k + 1))
                                V.tensor_scalar(S[:, k, :], iota[:, ds(win * P, P)], dstc[:, ds(TG * g + k, 1)], wc[:, ds(TG * g + k, 1)],
                                                ALU.is_equal, ALU.mult).then_inc(s_ready[l], 1)
                            dve.wait_ge(mm_done[l], TG * i + TG)
                            dve.wait_ge(acc_step[l], i + w + 1)
                            add_pair(l, (i + 1) % 2).then_inc(acc_step[l], 1)
                            dve.reg_mov(pend, win + ACC0)
                        dve.sem_inc(group_done[l], 1)
                done = dve.value_load(ctab[0:1, ds(g1, 1)], min_val=0, max_val=NG * NW)
                dve.wait_ge(mm_done[l], TG * done + TG)
                dve.wait_ge(acc_step[l], done + w + 1)
                add_pair(l, (done + 1) % 2).then_inc(acc_step[l], 1)
                dve.wait_ge(acc_step[l], done + w + 2)
                dve.sem_inc(flushed[l], 1)
                dve.reg_mov(pend, DUMMY)

            dve.wait_ge(root_turned, 1)
            link(V.tensor_copy(flat(rootT[:, :, :]), ps_dn[:, 0:D]))
            leaky(flat(rootT[:, :, :]), flat(rootT[:, :, :])).then_inc(root_kept, 1)
            dve.wait_ge(root_done, 1)
            V.tensor_copy(rootrow[:, :], ps_dn[:, 0:D]).then_inc(rootrow_ready, 1)
            dve.wait_ge(rootrow_ready, 1)

            dve.sem_inc(acc_step[0], 1)
            dve.sem_inc(group_done[0], RG)
            dve.sem_inc(z_ready[0], 1)
            dve.sem_inc(o_kept[0], 1)
            dve.sem_inc(t2_stored, 16)
            dve.sem_inc(agg_stored, 16)
            dve.reg_mov(pend, DUMMY)
            with dve.Fori(0, NI) as w:
                dve.wait_ge(o_done[0], w + 2)
                dve.wait_ge(t2_stored, 16 * (w + 1))
                V.tensor_tensor(rows[:, :], ps_o[:, 0:D], rootrow[:, :], op=ALU.add).then_inc(o_kept[0], 1)
                dve.wait_ge(staged[0], w + 1)
                V.tensor_copy(flat(acc[:, ds(w + (ACC0 - 1), 1), :]), zeros[:, :]).then_inc(acc_cleared, 1)
                edge_groups(0, w)
                dve.wait_ge(y_ready[0], w + 2)
                leaky(flat(zT[:, :, :]), flat(yT[:, :, :])).then_inc(z_ready[0], 1)

            dve.wait_ge(staged[0], NI + 1)
            V.memset(acc[:, ACC0 + NI - 1, :], 0.0).then_inc(acc_cleared, 1)
            dve.wait_ge(acc_cleared, NI + 1)
            dve.wait_ge(root_turned, 2)
            V.tensor_copy(flat(rootT[:, :, :]), ps_dn[:, 0:D]).then_inc(root_kept, 1)
            dve.wait_ge(root2_h, 1)
            for k in range(KC):
                last = V.tensor_scalar(root2T[:, k, :], ps_h[:, k * P:(k + 1) * P], b1c[:, k:k + 1], None, ALU.add)
            last.then_inc(root2_kept, 1)
            dve.wait_ge(root_done, 2)
            V.tensor_tensor(rootrow[:, :], ps_dn[:, 0:D], blb[:, :], op=ALU.add).then_inc(rootrow_ready, 1)
            dve.wait_ge(rootrow_ready, 2)
            for s in (acc_step[1], z_ready[1], o_kept[1], xn_ready, router_kept, down_kept):
                dve.sem_inc(s, 1)
            dve.sem_inc(group_done[1], RG)
            TAIL_LINKS = 5 + LN_LINKS
            with dve.Fori(0, NI) as w:
                dve.wait_ge(y_ready[1], w + 2)
                dve.wait_ge(o_done[1], w + 1)
                leaky(flat(zT[:, :, :]), flat(yT[:, :, :])).then_inc(z_ready[1], 1)
                dve.wait_ge(router_done, w + 1)
                V.tensor_scalar(wt[:, ds(w, 1)], ps_o[:, D:D + 1], brc[:, 0:1], None, ALU.add).then_inc(router_kept, 1)
                edge_groups(1, w)
                lk = Links(dve, ln_chain, w * TAIL_LINKS)
                xw = flat(xs[:, ds(w, 1), :])
                dve.wait_ge(o_done[1], w + 2)
                lk(V.tensor_tensor(vrow[:, :], ps_o[:, 0:D], rootrow[:, :], op=ALU.add))
                dve.sem_inc(o_kept[1], 1)
                lk(leaky(vrow[:, :], vrow[:, :]))
                lk(V.tensor_tensor(rows[:, :], xw, vrow[:, :], op=ALU.add))
                lk(V.bn_stats(bst[:, 0, :], rows[:, :]))
                dve.sem_inc(stats_held, 1)
                lk(V.bn_aggr(mv[:, 0, :], bst[:, 0, :]))
                inv_sqrt(lk, mv[:, 0, 1:2], ve[:, 0:1], nh[:, 0:1], ta[:, 0:1], rstd[:, 0:1])
                assert lk.steps == TAIL_LINKS
                dve.wait_ge(xnT_done, w + 2)
                V.tensor_scalar(xn[:, :], rows[:, :], mv[:, 0, 0:1], rstd[:, 0:1], ALU.subtract, ALU.mult).then_inc(xn_ready, 1)
                dve.wait_ge(xn_ready, w + 2)
                V.tensor_tensor(xw, rows[:, :], xn[:, :], op=ALU.add)
                dve.wait_ge(down_done, w + 2)
                V.tensor_tensor(flat(acc[:, ds(w, 1), :]), ps_dn[:, 0:D], fb2b[:, :], op=ALU.add).then_inc(down_kept, 1)

            lk = Links(dve, sel_chain)
            u = wt[:, SKEW:NI]
            cnt, tot = small[:, 0:1], ps_o[:, 0:1]
            pos, sign, limit, cut = (small[:, i:i + 1] for i in range(1, 5))
            dve.wait_ge(wt_masked, 1)
            dve.wait_ge(down_kept, NI + 1)
            V.tensor_scalar(scr[:, :], u, 0.0, 0.0, ALU.is_ge, ALU.add, accum_out=cnt).then_inc(count_ready, 1)
            lk(V.memset(thr[:, :], 0))
            lk(V.memset(bit[:, :], 1 << 30))
            dve.wait_ge(count_done, 1)
            lk(V.tensor_scalar(pos, tot, float(TOPK), None, ALU.is_ge))
            lk(V.tensor_scalar(sign, pos, 2.0, -1.0, ALU.mult, ALU.add))
            lk(V.tensor_scalar(limit, pos, float(NPAD - 2 * TOPK + 1), float(TOPK - 1), ALU.mult, ALU.add))
            lk(V.tensor_scalar(us[:, :], u, sign, None, ALU.mult))
            BITS, BIT_LINKS = 31, 4
            with dve.Fori(0, BITS) as r:
                bk = Links(dve, bit_chain, r * BIT_LINKS)
                bk(V.tensor_tensor(thr[:, 1:2], thr[:, 0:1], bit[:, :], op=ALU.bitwise_or))
                V.tensor_scalar(scr[:, :], us[:, :], thr[:, 1:2].bitcast(f32), 0.0, ALU.is_lt, ALU.add, accum_out=cnt).then_inc(count_ready, 1)
                dve.wait_ge(count_done, r + 2)
                bk(V.scalar_tensor_tensor(sel[:, :], tot, limit, bit[:, :], ALU.is_le, ALU.mult))
                bk(V.tensor_tensor(thr[:, 0:1], thr[:, 0:1], sel[:, :], op=ALU.bitwise_or))
                bk(V.tensor_scalar(bit[:, :], bit[:, :], 1, None, ALU.logical_shift_right))
                assert bk.steps == BIT_LINKS
            lk(V.tensor_scalar(cut, thr[:, 0:1].bitcast(f32), sign, None, ALU.mult))
            lk(V.tensor_scalar(mtie[:, :], u, cut, None, ALU.is_equal))
            dve.sem_inc(tie_ready, 1)
            lk(V.tensor_scalar(mgt[:, :], u, cut, 0.0, ALU.is_gt, ALU.add, accum_out=cnt))
            dve.sem_inc(count_ready, 1)
            dve.wait_ge(count_done, BITS + 2)
            left = pos
            lk(V.tensor_scalar(left, tot, -1.0, float(TOPK), ALU.mult, ALU.add))
            dve.wait_ge(tie_done, 1)
            lk(V.tensor_copy(scr[:, :], ps_h[:, 0:NW]))
            lk(V.memset(us[:, :], 0.0))
            lk(V.tensor_tensor_scan(mw[:, :], scr[:, :], us[:, :], 0.0, ALU.add, ALU.add))
            lk(V.tensor_tensor(mw[:, :], mw[:, :], scr[:, :], op=ALU.subtract))
            lk(V.tensor_tensor(mw[:, :], mw[:, :], ps_t[:, 0:NW], op=ALU.add))
            lk(V.scalar_tensor_tensor(mw[:, :], mw[:, :], left, mtie[:, :], ALU.is_lt, ALU.mult))
            lk(V.tensor_tensor(mw[:, :], mw[:, :], mgt[:, :], op=ALU.add))
            lk(V.tensor_tensor(mw[:, :], mw[:, :], u, op=ALU.mult))
            for c, (w0, w1) in enumerate(OUTCH):
                for w in range(w0, w1):
                    last = V.scalar_tensor_tensor(xs[:, X0 + w, :], acc[:, ACC0 + w, :], mw[:, w:w + 1], xs[:, X0 + w, :], ALU.mult, ALU.add)
                last.then_inc(out_ready, 1)


def kernel(x, src, dst, edge_weight, L0_gnn_W1, L0_gnn_b1, L0_gnn_W2, L0_gnn_b2, L0_gnn_Wl, L0_gnn_bl, L0_gnn_root_idx,
           L0_ffn_attention_mask, L0_ffn_wr, L0_ffn_br, L0_ffn_w1, L0_ffn_b1, L0_ffn_w2, L0_ffn_b2):
    import numpy as np
    from concourse import bacc
    from concourse.bass_utils import run_bass_kernel_spmd

    given = {
        "x": x, "src": src, "dst": dst, "edge_weight": edge_weight, "W1": L0_gnn_W1, "b1": L0_gnn_b1,
        "W2": L0_gnn_W2, "b2": L0_gnn_b2, "Wl": L0_gnn_Wl, "bl": L0_gnn_bl, "root_idx": L0_gnn_root_idx,
        "wr": L0_ffn_wr, "br": L0_ffn_br, "fw1": L0_ffn_w1, "fb1": L0_ffn_b1, "fw2": L0_ffn_w2, "fb2": L0_ffn_b2,
    }
    nc = bacc.Bacc("TRN2", target_bir_lowering=False, num_devices=1)
    arrays, aps = {}, {}
    for name, a in given.items():
        a = np.ascontiguousarray(a)
        arrays[f"in_{name}"] = a
        aps[name] = nc.dram_tensor(f"in_{name}", a.shape, mybir.dt.from_np(a.dtype), kind="ExternalInput").ap()
    aps["out"] = nc.dram_tensor("out_rows", tuple(np.shape(x)), mybir.dt.float32, kind="ExternalOutput").ap()
    gnn_ffn_kernel(nc, **aps)
    result = run_bass_kernel_spmd(nc, [arrays], core_ids=[0])
    return result.results[0]["out_rows"]
```
